# Optimizing a Trainium2 kernel written in Bass

```python
import numpy as np
import jax
import jax.numpy as jnp

def _softmax(x, axis=-1):
    return jax.nn.softmax(x, axis=axis)

def _gelu(x):
    return jax.nn.gelu(x, approximate=True)

def _silu(x):
    return jax.nn.silu(x)

def _sigmoid(x):
    return jax.nn.sigmoid(x)

def _layernorm(x, axis=-1, eps=1e-05):
    m = jnp.mean(x, axis=axis, keepdims=True)
    v = jnp.var(x, axis=axis, keepdims=True)
    return (x - m) / jnp.sqrt(v + eps)

def _scatter_add(tgt, idx, src, axis=0):
    return tgt.at[idx].add(src)

def _segment_sum(src, seg, n):
    return jax.ops.segment_sum(src, seg, n)
kernel_name = 'mk_adaln_ffn_d1_seqx_r4_86e2f0'

def setup_inputs(seed: int=0):
    np.random.seed(seed)
    _w = jnp.asarray

    def _rec_inputs():
        import jax
        import jax.numpy as jnp
        _rk = jax.random.key(seed)
        x = -7.109e-05 + 0.9999 * jax.random.normal(jax.random.fold_in(_rk, 1), (8, 256, 1024), jnp.float32)
        _lenS = 256 - jax.random.randint(jax.random.fold_in(_rk, 7), (8,), 0, max(1, 256 // 4) + 1, jnp.int32)
        _lenS2 = 256 - jax.random.randint(jax.random.fold_in(_rk, 8), (8,), 0, max(1, 256 // 4) + 1, jnp.int32)
        itok_B_0_15 = jax.random.randint(jax.random.fold_in(_rk, 11), (8,), 0, 16, jnp.int32)
        return (x, itok_B_0_15)
    x, itok_B_0_15 = _rec_inputs()

    def _L0_cond_setup():
        import jax, jax.numpy as jnp
        import numpy as np
        MAX_LORAS = 16
        IN, OUT = (1024, 1024)
        B, S = (8, 512)
        key = jax.random.key(seed)
        k1, k2, k3 = jax.random.split(key, 3)
        x = jax.random.normal(k1, (B, S, IN), dtype=jnp.float32)
        adapter_ids = jax.random.randint(k2, (B,), 0, MAX_LORAS)
        weight = jax.random.normal(k3, (MAX_LORAS, OUT, IN), dtype=jnp.float32) * 0.02
        return {'x': x, 'adapter_ids': adapter_ids, 'weight': weight}
    _L0_cond_all = _L0_cond_setup()
    _L0_cond_in = {k: v for k, v in _L0_cond_all.items() if k in ('weight',)}
    del _L0_cond_all

    def _L0_ffn_setup():
        import jax, jax.numpy as jnp
        import numpy as np
        B, L, H, Dh, M = (4, 512, 16, 64, 256)
        D = H * Dh
        key = jax.random.key(seed)
        kx, ku, kd, kp = jax.random.split(key, 4)
        x = jax.random.normal(kx, (B, L, D), dtype=jnp.float32)
        up = jax.random.normal(ku, (H, Dh, M), dtype=jnp.float32)
        down = jax.random.normal(kd, (H, M, Dh), dtype=jnp.float32)
        perm = jax.random.permutation(kp, D)
        return {'x': x, 'up': up, 'down': down, 'perm': perm}
    _L0_ffn_all = _L0_ffn_setup()
    _L0_ffn_in = {k: v for k, v in _L0_ffn_all.items() if k in ('up', 'down', 'perm')}
    del _L0_ffn_all
    return {'x': x, 'itok_B_0_15': itok_B_0_15, 'L0_cond_weight': _L0_cond_in['weight'], 'L0_ffn_up': _L0_ffn_in['up'], 'L0_ffn_down': _L0_ffn_in['down'], 'L0_ffn_perm': _L0_ffn_in['perm']}

def reference(x, itok_B_0_15, L0_cond_weight, L0_ffn_up, L0_ffn_down, L0_ffn_perm):
    import jax
    import jax.numpy as jnp

    def _L0_cond_ref(x, adapter_ids, weight):
        import jax, jax.numpy as jnp
        import numpy as np
        MAX_LORAS = 16
        IN, OUT = (1024, 1024)
        B, S = (8, 512)
        w = weight[adapter_ids]
        return jnp.einsum('bsi,boi->bso', x, w)

    def _L0_ffn_ref(x, up, down, perm):
        import jax, jax.numpy as jnp
        import numpy as np
        B, L, H, Dh, M = (4, 512, 16, 64, 256)
        D = H * Dh
        b, l, Dm = x.shape
        h, d = (up.shape[0], up.shape[1])
        unperm = jnp.argsort(perm)
        t = x.reshape(b * l, Dm)
        t = t[:, perm]
        t = t.reshape(b * l, h, d)
        t = jnp.einsum('bhd,hdm->bhm', t, up)
        t = jax.nn.gelu(t, approximate=False)
        t = jnp.einsum('bhm,hmd->bhd', t, down)
        t = t.reshape(b * l, h * d)
        t = t[:, unperm]
        out = t.reshape(b, l, Dm)
        return out
    x = x + _L0_ffn_ref(_L0_cond_ref(x, itok_B_0_15, L0_cond_weight), L0_ffn_up, L0_ffn_down, L0_ffn_perm)
    return x

_drawn_inputs = setup_inputs


def setup_inputs(seed=0):
    import zlib

    import numpy as np

    out = dict(_drawn_inputs(seed))
    spreads = {}
    factors = {}
    for name, (base, spread) in spreads.items():
        noise = np.random.default_rng([zlib.crc32(name.encode()), seed]).standard_normal(out[name].shape)
        drawn = base * np.exp(spread * noise) if base else spread * noise
        out[name] = jnp.asarray(drawn.astype(out[name].dtype))
    for name, factor in factors.items():
        out[name] = (out[name] * factor).astype(out[name].dtype)
    return out
```

```python
from contextlib import ExitStack

import numpy as np

import concourse.bass as bass
from concourse import mybir

F32 = mybir.dt.float32
F32R = mybir.dt.float32r
I32 = mybir.dt.int32
ALU = mybir.AluOpType
ACT = mybir.ActivationFunctionType

P = 128
B, S, D = 8, 256, 1024
NW = 16
H, DH, M = 16, 64, 256
KT = D // P
OU = 256
OT = OU // P
LPB = D // OU
BC = 2
CH = B // BC
TOK = BC * S
LU = BC * LPB
FU = H // 2
MT = M // P
HALF = KT // 2

WRAW, WS, XS = 4, 2, 2
TG, SS, HS, XR, YS = 4, 2, 2, 8, 2
LAG = 3

PROLOGUE = [("L", i) for i in range(LU)]
BODY = [("L", 0)]
for _i in range(1, LU):
    BODY += [("L", _i), ("F", _i - 1)]
BODY += [("F", FU - 1)]
EPILOGUE = [("F", i) for i in range(FU)]


def build(nc, x_cols, x_rows, w, up, down, perm, ids, out_rows):
    y_rows = nc.dram_tensor("y_rows", [CH * D, TOK], F32, kind="Internal").ap()

    ctx = ExitStack()
    with ctx:
        def sb(name, shape, dt):
            return ctx.enter_context(nc.sbuf_tensor(name, shape, dt))

        def pb(name, shape):
            return ctx.enter_context(nc.psum_tensor(name, shape, F32))

        def sem(name):
            return ctx.enter_context(nc.semaphore(name))

        ids_sb = sb("ids_sb", [1, B], I32)
        idx = sb("idx", [P, CH, FU], I32)
        w_raw = sb("w_raw", [P, WRAW, KT, OU], F32)
        w_hi = sb("w_hi", [P, WS, KT, OU], F32R)
        w_lo = sb("w_lo", [P, WS, KT, OU], F32R)
        x_raw = sb("x_raw", [P, KT, S], F32)
        x_hi = sb("x_hi", [P, XS, KT, S], F32R)
        x_lo = sb("x_lo", [P, XS, KT, S], F32R)
        up_hi = sb("up_hi", [P, H, M], F32R)
        up_lo = sb("up_lo", [P, H, M], F32R)
        down_sb = sb("down_sb", [P, H, MT, DH], F32)
        y_out = sb("y_out", [P, YS, OT, S], F32)
        t_raw = sb("t_raw", [P, TG, TOK], F32)
        t_split = sb("t_split", [P, SS, 2, TOK], F32R)
        hidden = sb("hidden", [P, HS, 2, MT, TOK], F32)
        rows = sb("rows", [P, XR, TOK], F32)
        up_raw = hidden[:, :, :, :, :].rearrange("p s h m t -> p (s h m t)").rearrange("p (h m) -> p h m", h=H)

        ps_y = [pb(f"ps_y{i}", [P, OT, S]) for i in range(2)]
        ps_up = [pb(f"ps_up{i}", [P, MT, TOK]) for i in range(2)]
        ps_dn = [pb(f"ps_dn{i}", [P, TOK]) for i in range(2)]

        ids_in = sem("ids_in")
        perm_in = sem("perm_in")
        w_in = [sem(f"w_in{i}") for i in range(WRAW)]
        x_in = sem("x_in")
        up_in = sem("up_in")
        down_in = sem("down_in")
        y_parked = [sem(f"y_parked{i}") for i in range(YS)]
        t_in = [sem(f"t_in{i}") for i in range(TG)]
        rows_in = [sem(f"rows_in{i}") for i in range(XR)]
        out_written = [sem(f"out_written{i}") for i in range(XR)]
        idx_ready = sem("idx_ready")
        w_hi_done = sem("w_hi_done")
        w_lo_done = sem("w_lo_done")
        x_hi_done = sem("x_hi_done")
        x_lo_done = sem("x_lo_done")
        up_hi_done = sem("up_hi_done")
        up_lo_done = sem("up_lo_done")
        lora_done = sem("lora_done")
        y_copied = sem("y_copied")
        t_hi_done = sem("t_hi_done")
        t_lo_done = sem("t_lo_done")
        up_done = sem("up_done")
        gelu_done = sem("gelu_done")
        down_done = sem("down_done")
        added = sem("added")

        block = ctx.enter_context(nc.Block())

        def over_chunks(eng, steps):
            steps(0, None, True)
            with eng.Fori(1, CH - 1) as c:
                steps(c, c - 1, True)
            steps(CH - 1, CH - 2, False)
            steps(None, CH - 1, False)

        def plan(lora, ffn):
            return BODY if lora is not None and ffn is not None else PROLOGUE if ffn is None else EPILOGUE

        @block.sync
        def _(sp):
            sp.dma_start(ids_sb[:, :], ids).then_inc(ids_in, 16)
            sp.dma_start(idx[:, 0, :], perm).then_inc(perm_in, 16)
            sp.wait_ge(ids_in, 16)

            def loads(chunk):
                for r in range(BC):
                    b = BC * chunk + r
                    if not isinstance(b, int) or b > 0:
                        sp.wait_ge(x_lo_done, b)
                    sp.dma_start(x_raw[:, :, :], x_cols[bass.ds(b, 1), :, :, :].rearrange("a p k s -> (a p) k s")).then_inc(x_in, 16)
                    adapter = sp.value_load(ids_sb[0:1, bass.ds(b, 1)], min_val=0, max_val=NW - 1)
                    for q in range(LPB):
                        i = LPB * r + q
                        g = LU * chunk + i
                        if not isinstance(g, int) or g >= WRAW:
                            sp.wait_ge(w_lo_done, 2 * (g - WRAW + 1))
                        sp.dma_start(w_raw[:, i % WRAW, :, :],
                                     w[bass.ds(adapter * LPB + q, 1), :, :, :].rearrange("a p k o -> (a p) k o")).then_inc(w_in[i % WRAW], 16)

            loads(0)
            for part in range(2):
                sp.dma_start(up_raw[part * DH:(part + 1) * DH, :, :], up).then_inc(up_in, 16)
            sp.dma_start(down_sb[:, :, :, :], down).then_inc(down_in, 16)
            with sp.Fori(1, CH) as chunk:
                loads(chunk)

        @block.gpsimd
        def _(pool):
            pool.wait_ge(perm_in, 16)
            for chunk in range(1, CH):
                nc.gpsimd.tensor_scalar(idx[:, chunk, :], idx[:, 0, :], D * chunk, None, ALU.add).then_inc(idx_ready, 1)
            pool.wait_ge(idx_ready, CH - 1)

            for chunk in range(CH):
                def rows_of(i):
                    return bass.IndirectOffsetOnAxis(ap=idx[:, chunk, i:i + 1], axis=0)

                def scatter(i):
                    pool.wait_ge(added, FU * chunk + i + 1)
                    nc.gpsimd.indirect_dma_start(out_rows, rows_of(i), rows[:, i, :], None).then_inc(out_written[i], 16)

                for s in range(YS):
                    pool.wait_ge(y_parked[s], 16 * (LU // YS) * (chunk + 1))
                for i in range(FU):
                    f = FU * chunk + i
                    if f >= TG:
                        pool.wait_ge(t_lo_done, f - TG + 1)
                    nc.gpsimd.indirect_dma_start(t_raw[:, i % TG, :], None, y_rows[0:D * (chunk + 1), :], rows_of(i)).then_inc(t_in[i % TG], 16)
                    if chunk > 0:
                        pool.wait_ge(out_written[i], 16 * chunk)
                    nc.gpsimd.indirect_dma_start(rows[:, i, :], None, x_rows, rows_of(i)).then_inc(rows_in[i], 16)
                    if i >= LAG:
                        scatter(i - LAG)
                for i in range(FU - LAG, FU):
                    scatter(i)
            for s in range(XR):
                pool.wait_ge(out_written[s], 16 * CH)

        @block.scalar
        def _(act):
            def w_high(chunk, i):
                g = LU * chunk + i
                act.wait_ge(w_in[i % WRAW], 16 * ((LU // WRAW) * chunk + i // WRAW + 1))
                if not isinstance(g, int) or g >= WS:
                    act.wait_ge(lora_done, g - WS + 1)
                for n in range(2):
                    k = slice(n * HALF, (n + 1) * HALF)
                    nc.scalar.activation(w_hi[:, i % WS, k, :], w_raw[:, i % WRAW, k, :], ACT.Copy).then_inc(w_hi_done, 1)

            def x_high(b, slot):
                act.wait_ge(x_in, 16 * (b + 1))
                if not isinstance(b, int) or b >= XS:
                    act.wait_ge(lora_done, LPB * (b - XS + 1))
                nc.scalar.activation(x_hi[:, slot, :, :], x_raw[:, :, :], ACT.Copy).then_inc(x_hi_done, 1)

            def y_away(chunk, i):
                g = LU * chunk + i
                row, tok = (i % LPB) * OU, (i // LPB) * S
                act.wait_ge(lora_done, g + 1)
                if not isinstance(g, int) or g >= YS:
                    act.wait_ge(y_parked[i % YS], 16 * ((LU // YS) * chunk + i // YS))
                nc.scalar.activation(y_out[:, i % YS, :, :], ps_y[i % 2][:, :, :], ACT.Copy).then_inc(y_copied, 1)
                act.wait_ge(y_copied, g + 1)
                act.dma_start(y_rows[bass.ds(D * chunk + row, OU), tok:tok + S].rearrange("(o p) s -> p o s", o=OT),
                              y_out[:, i % YS, :, :]).then_inc(y_parked[i % YS], 16)

            def t_high(chunk, i):
                act.wait_ge(t_in[i % TG], 16 * ((FU // TG) * chunk + i // TG + 1))
                if i >= SS:
                    act.wait_ge(up_done, 2 * (FU * chunk + i - SS + 1))
                nc.scalar.activation(t_split[0:DH, i % SS, 0, :], t_raw[0:DH, i % TG, :], ACT.Copy).then_inc(t_hi_done, 1)
                nc.scalar.activation(t_split[DH:P, i % SS, 1, :], t_raw[DH:P, i % TG, :], ACT.Copy).then_inc(t_hi_done, 1)

            def gelu(chunk, i):
                if i >= HS:
                    act.wait_ge(down_done, FU * chunk + i - HS + 1)
                elif isinstance(chunk, int):
                    act.wait_ge(down_done, FU * chunk)
                for h in range(2):
                    act.wait_ge(up_done, 2 * (FU * chunk + i) + h + 1)
                    nc.scalar.activation(hidden[:, i % HS, h, :, :], ps_up[h][:, :, :], ACT.Gelu).then_inc(gelu_done, 1)

            x_high(0, 0)
            w_high(0, 0)

            def steps(lora, ffn, more):
                if lora is None:
                    t_high(ffn, 0)
                for kind, i in plan(lora, ffn):
                    if kind == "L":
                        if i + 1 < LU:
                            w_high(lora, i + 1)
                        elif more:
                            w_high(lora + 1, 0)
                        if i == 2:
                            x_high(BC * lora + 1, 1)
                        if i == 2 + LPB and more:
                            x_high(BC * lora + 2, 0)
                        if ffn is not None and i == 1:
                            t_high(ffn, 0)
                        y_away(lora, i)
                        if ffn is None and i in (3, 4):
                            act.wait_ge(up_in, 32)
                            h = slice((i - 3) * H // 2, (i - 2) * H // 2)
                            nc.scalar.activation(up_hi[:, h, :], up_raw[:, h, :], ACT.Copy).then_inc(up_hi_done, 1)
                    else:
                        if i + 1 < FU:
                            t_high(ffn, i + 1)
                        if not isinstance(ffn, int):
                            act.wait_ge(up_lo_done, 2)
                        gelu(ffn, i)

            over_chunks(act, steps)

        @block.vector
        def _(dve):
            def w_low(chunk, i):
                g = LU * chunk + i
                for n in range(2):
                    k = slice(n * HALF, (n + 1) * HALF)
                    dve.wait_ge(w_hi_done, 2 * g + n + 1)
                    nc.vector.tensor_tensor(w_lo[:, i % WS, k, :], w_raw[:, i % WRAW, k, :],
                                            w_hi[:, i % WS, k, :].bitcast(F32), ALU.subtract).then_inc(w_lo_done, 1)

            def x_low(b, slot):
                dve.wait_ge(x_hi_done, b + 1)
                nc.vector.tensor_tensor(x_lo[:, slot, :, :], x_raw[:, :, :], x_hi[:, slot, :, :].bitcast(F32),
                                        ALU.subtract).then_inc(x_lo_done, 1)

            def t_low(chunk, i):
                f = FU * chunk + i
                dve.wait_ge(t_hi_done, 2 * (f + 1))
                nc.vector.tensor_tensor(t_split[DH:P, i % SS, 0, :], t_raw[0:DH, i % TG, :],
                                        t_split[0:DH, i % SS, 0, :].bitcast(F32), ALU.subtract)
                nc.vector.tensor_tensor(t_split[0:DH, i % SS, 1, :], t_raw[DH:P, i % TG, :],
                                        t_split[DH:P, i % SS, 1, :].bitcast(F32), ALU.subtract).then_inc(t_lo_done, 1)

            def add_x(chunk, i):
                f = FU * chunk + i
                dve.wait_ge(rows_in[i], 16 * (chunk + 1))
                dve.wait_ge(down_done, f + 1)
                nc.vector.tensor_tensor(rows[:, i, :], ps_dn[i % 2][:, :], rows[:, i, :], ALU.add).then_inc(added, 1)

            x_low(0, 0)
            w_low(0, 0)

            def steps(lora, ffn, more):
                if lora is None:
                    t_low(ffn, 0)
                for kind, i in plan(lora, ffn):
                    if kind == "L":
                        if i + 1 < LU:
                            w_low(lora, i + 1)
                        elif more:
                            w_low(lora + 1, 0)
                        if i == 2:
                            x_low(BC * lora + 1, 1)
                        if i == 2 + LPB and more:
                            x_low(BC * lora + 2, 0)
                        if ffn is not None and i == 1:
                            t_low(ffn, 0)
                        if ffn is None and i in (3, 4):
                            dve.wait_ge(up_hi_done, i - 2)
                            h = slice((i - 3) * H // 2, (i - 2) * H // 2)
                            nc.vector.tensor_tensor(up_lo[:, h, :], up_raw[:, h, :], up_hi[:, h, :].bitcast(F32),
                                                    ALU.subtract).then_inc(up_lo_done, 1)
                    else:
                        if i + 1 < FU:
                            t_low(ffn, i + 1)
                        if i > 0:
                            add_x(ffn, i - 1)
                if ffn is not None:
                    add_x(ffn, FU - 1)

            over_chunks(dve, steps)

        @block.tensor
        def _(pe):
            def lora_unit(chunk, i):
                g = LU * chunk + i
                xs, ws = i // LPB, i % WS
                if i % LPB == 0:
                    pe.wait_ge(x_lo_done, BC * chunk + xs + 1)
                if not isinstance(g, int) or g >= 2:
                    pe.wait_ge(y_copied, g - 1)
                for o in range(OT):
                    col = slice(o * P, (o + 1) * P)
                    for k in range(KT):
                        if o == 0 and k % HALF == 0:
                            pe.wait_ge(w_lo_done, 2 * g + k // HALF + 1)
                        acc = ps_y[i % 2][:, o, :]
                        nc.tensor.matmul(acc, w_hi[:, ws, k, col], x_hi[:, xs, k, :], start=(k == 0), stop=False)
                        nc.tensor.matmul(acc, w_hi[:, ws, k, col], x_lo[:, xs, k, :], start=False, stop=False)
                        last = nc.tensor.matmul(acc, w_lo[:, ws, k, col], x_hi[:, xs, k, :], start=False, stop=(k == KT - 1))
                last.then_inc(lora_done, 1)

            def up_unit(chunk, i):
                f = FU * chunk + i
                pe.wait_ge(t_lo_done, f + 1)
                for h in range(2):
                    if i > 0:
                        pe.wait_ge(gelu_done, 2 * (FU * chunk + i - 1) + h + 1)
                    for m in range(MT):
                        col = slice(m * P, (m + 1) * P)
                        nc.tensor.matmul(ps_up[h][:, m, :], up_hi[:, 2 * i + h, col], t_split[:, i % SS, h, :], start=True, stop=False)
                        last = nc.tensor.matmul(ps_up[h][:, m, :], up_lo[:, 2 * i + h, col], t_split[:, i % SS, h, :], start=False, stop=True)
                    last.then_inc(up_done, 1)

            def down_unit(chunk, i):
                f = FU * chunk + i
                pe.wait_ge(gelu_done, 2 * (f + 1))
                if i > 1:
                    pe.wait_ge(added, FU * chunk + i - 1)
                for m in range(MT):
                    for h in range(2):
                        last = nc.tensor.matmul(ps_dn[i % 2][h * DH:(h + 1) * DH, :], down_sb[:, 2 * i + h, m, :],
                                                hidden[:, i % HS, h, m, :], start=(m == 0), stop=(m == MT - 1))
                last.then_inc(down_done, 1)

            def steps(lora, ffn, more):
                for kind, i in plan(lora, ffn):
                    if kind == "L":
                        lora_unit(lora, i)
                    else:
                        up_unit(ffn, i)
                        if i > 0:
                            down_unit(ffn, i - 1)
                if ffn is None:
                    pe.wait_ge(up_lo_done, 2)
                    pe.wait_ge(down_in, 16)
                else:
                    down_unit(ffn, FU - 1)

            over_chunks(pe, steps)


def kernel(x, itok_B_0_15, L0_cond_weight, L0_ffn_up, L0_ffn_down, L0_ffn_perm):
    import concourse.bacc as bacc
    from concourse.bass_utils import run_bass_kernel_spmd

    x, w = np.asarray(x), np.asarray(L0_cond_weight)
    up, down = np.asarray(L0_ffn_up), np.asarray(L0_ffn_down)
    perm, ids = np.asarray(L0_ffn_perm), np.asarray(itok_B_0_15)
    arrays = {
        "x_cols": x.reshape(B, S, KT, P).transpose(0, 3, 2, 1),
        "x_rows": x.reshape(CH, BC, S, D).transpose(0, 3, 1, 2).reshape(CH * D, TOK),
        "w": w.reshape(NW * LPB, OU, KT, P).transpose(0, 3, 2, 1),
        "up": up.transpose(1, 0, 2),
        "down": down.reshape(H, MT, P, DH).transpose(2, 0, 1, 3),
        "perm": perm.reshape(FU, P).T,
        "ids": ids.reshape(1, B),
    }
    arrays = {n: np.ascontiguousarray(a) for n, a in arrays.items()}
    nc = bacc.Bacc("TRN2", target_bir_lowering=False, num_devices=1)
    aps = [nc.dram_tensor(n, a.shape, mybir.dt.from_np(a.dtype), kind="ExternalInput").ap() for n, a in arrays.items()]
    out = nc.dram_tensor("out_rows", [CH * D, TOK], F32, kind="ExternalOutput").ap()
    build(nc, *aps, out)
    got = run_bass_kernel_spmd(nc, [arrays], core_ids=[0]).results[0]["out_rows"]
    return got.reshape(CH, D, BC, S).transpose(0, 2, 3, 1).reshape(B, S, D)
```

```python
from contextlib import ExitStack

import numpy as np

import concourse.bass as bass
from concourse import mybir

F32 = mybir.dt.float32
F32R = mybir.dt.float32r
I32 = mybir.dt.int32
ALU = mybir.AluOpType
ACT = mybir.ActivationFunctionType

P = 128
B, S, D = 8, 256, 1024
NW = 16
H, DH, M = 16, 64, 256
KT = D // P
OU = 256
OT = OU // P
LPB = D // OU
BC = 2
CH = B // BC
TOK = BC * S
LU = BC * LPB
FU = H // 2
MT = M // P
HALF = KT // 2
FIRST = [(0, 1), (1, 3), (3, 5), (5, KT)]
PIECES = len(FIRST)

WRAW, WS, XS = 4, 2, 2
TG, SS, HS, XR, YS = 4, 2, 2, 8, 2
LAG = 4

PROLOGUE = [("L", i) for i in range(LU)]
LEAD = 3
BODY = [("L", i) for i in range(LEAD)]
for _i in range(LEAD, LU):
    BODY += [("L", _i), ("F", _i - LEAD)]
BODY += [("F", i) for i in range(LU - LEAD, FU)]
X_STEPS = (1, 5)
X_STEPS_FIRST = (2, 6)
UP_STEPS = (5, 7)
UP_AT, DOWN_AT = 3, 7
HELD = 3
LAST_BODY = [step for step in BODY if step[0] == "L" or step[1] < FU - HELD] + [("F", i) for i in range(FU - HELD, FU)]
EPILOGUE = [("F", i) for i in range(FU)]


def build(nc, x_cols, x_rows, w, up, down, perm, ids, out_rows):
    y_rows = nc.dram_tensor("y_rows", [CH * D, TOK], F32, kind="Internal").ap()

    ctx = ExitStack()
    with ctx:
        def sb(name, shape, dt):
            return ctx.enter_context(nc.sbuf_tensor(name, shape, dt))

        def pb(name, shape):
            return ctx.enter_context(nc.psum_tensor(name, shape, F32))

        def sem(name):
            return ctx.enter_context(nc.semaphore(name))

        idx = sb("idx", [P, CH, FU], I32)
        w_raw = sb("w_raw", [P, WRAW, KT, OU], F32)
        w_hi = sb("w_hi", [P, WS, KT, OU], F32R)
        w_lo = sb("w_lo", [P, WS, KT, OU], F32R)
        x_raw = sb("x_raw", [P, KT, S], F32)
        x_hi = sb("x_hi", [P, XS, KT, S], F32R)
        x_lo = sb("x_lo", [P, XS, KT, S], F32R)
        up_hi = sb("up_hi", [P, H, M], F32R)
        up_lo = sb("up_lo", [P, H, M], F32R)
        down_sb = sb("down_sb", [P, H, MT, DH], F32)
        y_out = sb("y_out", [P, YS, OT, S], F32)
        t_raw = sb("t_raw", [P, TG, TOK], F32)
        t_split = sb("t_split", [P, SS, 2, TOK], F32R)
        hidden = sb("hidden", [P, HS, 2, MT, TOK], F32)
        rows = sb("rows", [P, XR, TOK], F32)
        up_raw = hidden[:, 0, :, :, :].rearrange("p h m t -> p (h m t)").rearrange("p (h m) -> p h m", h=H // 2)

        ps_y = [pb(f"ps_y{i}", [P, OT, S]) for i in range(2)]
        ps_up = [pb(f"ps_up{i}", [P, MT, TOK]) for i in range(2)]
        ps_dn = [pb(f"ps_dn{i}", [P, TOK]) for i in range(2)]

        perm_in = sem("perm_in")
        w_in = [sem(f"w_in{i}") for i in range(WRAW)]
        x_in = sem("x_in")
        first_w_in = [sem(f"first_w_in{n}") for n in range(PIECES)]
        first_x_in = [sem(f"first_x_in{n}") for n in range(PIECES)]
        up_in = sem("up_in")
        down_in = sem("down_in")
        y_parked = [sem(f"y_parked{i}") for i in range(YS)]
        t_in = [sem(f"t_in{i}") for i in range(TG)]
        rows_in = [sem(f"rows_in{i}") for i in range(XR)]
        out_written = [sem(f"out_written{i}") for i in range(XR)]
        first_w_hi = sem("first_w_hi")
        first_w_lo = sem("first_w_lo")
        first_x_hi = sem("first_x_hi")
        first_x_lo = sem("first_x_lo")
        idx_ready = sem("idx_ready")
        w_hi_done = sem("w_hi_done")
        w_lo_done = sem("w_lo_done")
        x_hi_done = sem("x_hi_done")
        x_lo_done = sem("x_lo_done")
        up_hi_done = sem("up_hi_done")
        up_lo_own = sem("up_lo_own")
        up_hi_other = sem("up_hi_other")
        up_lo_other = sem("up_lo_other")
        lora_done = sem("lora_done")
        y_copied = sem("y_copied")
        t_hi_done = sem("t_hi_done")
        t_lo_done = sem("t_lo_done")
        up_done = sem("up_done")
        gelu_done = sem("gelu_done")
        down_done = sem("down_done")
        added = sem("added")

        block = ctx.enter_context(nc.Block())

        def over_chunks(eng, steps):
            steps(0, None, True)
            with eng.Fori(1, CH - 1) as c:
                steps(c, c - 1, True)
            steps(CH - 1, CH - 2, False)
            steps(None, CH - 1, False)

        def up_half(half):
            below, above = slice(0, DH), slice(DH, P)
            heads = slice(half * H // 2, (half + 1) * H // 2)
            return (heads, below, above) if half == 0 else (heads, above, below)

        def last_body(lora):
            return isinstance(lora, int) and lora == CH - 1

        def plan(lora, ffn):
            if lora is None or ffn is None:
                return PROLOGUE if ffn is None else EPILOGUE
            return LAST_BODY if isinstance(lora, int) else BODY

        @block.sync
        def _(sp):
            def adapter_of(b):
                return sp.value_load(ids[0:1, bass.ds(b, 1)], min_val=0, max_val=NW - 1)

            def load_x(b):
                if isinstance(b, int) and b == 1:
                    sp.wait_ge(first_x_lo, PIECES)
                else:
                    sp.wait_ge(x_lo_done, b - 1)
                sp.dma_start(x_raw[:, :, :], x_cols[bass.ds(b, 1), :, :, :].rearrange("a p k s -> (a p) k s")).then_inc(x_in, 16)

            def load_w(chunk, i, adapter):
                g = LU * chunk + i
                if isinstance(g, int) and g == WRAW:
                    sp.wait_ge(first_w_lo, PIECES)
                elif not isinstance(g, int) or g > WRAW:
                    sp.wait_ge(w_lo_done, 2 * (g - WRAW))
                sp.dma_start(w_raw[:, i % WRAW, :, :],
                             w[bass.ds(adapter * LPB + i % LPB, 1), :, :, :].rearrange("a p k o -> (a p) k o")
                             ).then_inc(w_in[i % WRAW], 16)

            adapter = adapter_of(0)
            for n in range(PIECES):
                k = slice(*FIRST[n])
                sp.dma_start(w_raw[:, 0, k, :],
                             w[bass.ds(adapter * LPB, 1), :, k, :].rearrange("a p k o -> (a p) k o")).then_inc(first_w_in[n], 16)
            for i in range(1, LPB):
                load_w(0, i, adapter)
            load_x(1)
            adapter = adapter_of(1)
            for i in range(LPB, LU):
                load_w(0, i, adapter)
            with sp.Fori(1, CH) as chunk:
                for r in range(BC):
                    load_x(BC * chunk + r)
                    adapter = adapter_of(BC * chunk + r)
                    for i in range(LPB * r, LPB * (r + 1)):
                        load_w(chunk, i, adapter)

        @block.gpsimd
        def _(pool):
            pool.dma_start(idx[:, 0, :], perm).then_inc(perm_in, 16)
            for n in range(PIECES):
                k = slice(*FIRST[n])
                pool.wait_ge(first_x_hi, n + 1)
                nc.gpsimd.tensor_tensor(x_lo[:, 0, k, :], x_raw[:, k, :], x_hi[:, 0, k, :].bitcast(F32),
                                        ALU.subtract).then_inc(first_x_lo, 1)
            pool.wait_ge(perm_in, 16)
            for chunk in range(1, CH):
                nc.gpsimd.tensor_scalar(idx[:, chunk, :], idx[:, 0, :], D * chunk, None, ALU.add).then_inc(idx_ready, 1)
            pool.wait_ge(idx_ready, CH - 1)

            pool.wait_ge(lora_done, UP_AT)
            pool.dma_start(up_raw[:, :, :], up).then_inc(up_in, 16)
            for half in range(2):
                heads, own, other = up_half(half)
                pool.wait_ge(up_hi_done, half + 1)
                nc.gpsimd.tensor_tensor(up_lo[own, heads, :], up_raw[own, :, :], up_hi[own, heads, :].bitcast(F32),
                                        ALU.subtract).then_inc(up_lo_own, 1)
            pool.wait_ge(lora_done, DOWN_AT)
            pool.dma_start(down_sb[:, :, :, :], down).then_inc(down_in, 16)
            pool.wait_ge(up_lo_own, 2)

            def rows_of(f):
                return bass.IndirectOffsetOnAxis(ap=idx[:, f // FU, f % FU:f % FU + 1], axis=0)

            def scatter(f):
                pool.wait_ge(added, f + 1)
                nc.gpsimd.indirect_dma_start(out_rows, rows_of(f), rows[:, f % XR, :], None).then_inc(out_written[f % XR], 16)

            for f in range(CH * FU):
                chunk = f // FU
                if f % FU == 0:
                    for s in range(YS):
                        pool.wait_ge(y_parked[s], 16 * (LU // YS) * (chunk + 1))
                if f >= TG:
                    pool.wait_ge(t_lo_done, f - TG + 1)
                nc.gpsimd.indirect_dma_start(t_raw[:, f % TG, :], None, y_rows[0:D * (chunk + 1), :],
                                             rows_of(f)).then_inc(t_in[f % TG], 16)
                if f >= XR:
                    pool.wait_ge(out_written[f % XR], 16 * (f // XR))
                nc.gpsimd.indirect_dma_start(rows[:, f % XR, :], None, x_rows, rows_of(f)).then_inc(rows_in[f % XR], 16)
                if f >= LAG:
                    scatter(f - LAG)
            for f in range(CH * FU - LAG, CH * FU):
                scatter(f)
            for s in range(XR):
                pool.wait_ge(out_written[s], 16 * CH)

        @block.scalar
        def _(act):
            def w_high(chunk, i):
                g = LU * chunk + i
                act.wait_ge(w_in[i % WRAW], 16 * ((LU // WRAW) * chunk + i // WRAW + (i % WRAW > 0)))
                if not isinstance(g, int) or g >= WS:
                    act.wait_ge(lora_done, g - WS + 1)
                for n in range(2):
                    k = slice(n * HALF, (n + 1) * HALF)
                    nc.scalar.activation(w_hi[:, i % WS, k, :], w_raw[:, i % WRAW, k, :], ACT.Copy).then_inc(w_hi_done, 1)

            def x_high(b, slot):
                act.wait_ge(x_in, 16 * b)
                if not isinstance(b, int) or b >= XS:
                    act.wait_ge(lora_done, LPB * (b - XS + 1))
                nc.scalar.activation(x_hi[:, slot, :, :], x_raw[:, :, :], ACT.Copy).then_inc(x_hi_done, 1)

            def y_copy(chunk, i):
                g = LU * chunk + i
                act.wait_ge(lora_done, g + 1)
                if not isinstance(g, int) or g >= YS:
                    act.wait_ge(y_parked[i % YS], 16 * ((LU // YS) * chunk + i // YS))
                if isinstance(g, int) and g == 0:
                    nc.scalar.activation(y_out[:, 0, 0, :], ps_y[0][:, 0, :], ACT.Copy)
                    nc.scalar.activation(y_out[:, 0, 1, :], ps_dn[0][:, 0:S], ACT.Copy).then_inc(y_copied, 1)
                else:
                    nc.scalar.activation(y_out[:, i % YS, :, :], ps_y[i % 2][:, :, :], ACT.Copy).then_inc(y_copied, 1)

            def y_park(chunk, i):
                row, tok = (i % LPB) * OU, (i // LPB) * S
                act.wait_ge(y_copied, LU * chunk + i + 1)
                act.dma_start(y_rows[bass.ds(D * chunk + row, OU), tok:tok + S].rearrange("(o p) s -> p o s", o=OT),
                              y_out[:, i % YS, :, :]).then_inc(y_parked[i % YS], 16)

            def t_high(chunk, i):
                act.wait_ge(t_in[i % TG], 16 * ((FU // TG) * chunk + i // TG + 1))
                if i >= SS or isinstance(chunk, int):
                    act.wait_ge(up_done, 2 * (FU * chunk + i - SS + 1))
                nc.scalar.activation(t_split[0:DH, i % SS, 0, :], t_raw[0:DH, i % TG, :], ACT.Copy).then_inc(t_hi_done, 1)
                nc.scalar.activation(t_split[DH:P, i % SS, 1, :], t_raw[DH:P, i % TG, :], ACT.Copy).then_inc(t_hi_done, 1)

            def gelu(chunk, i):
                if i >= HS:
                    act.wait_ge(down_done, FU * chunk + i - HS + 1)
                elif isinstance(chunk, int):
                    act.wait_ge(down_done, FU * chunk)
                for h in range(2):
                    act.wait_ge(up_done, 2 * (FU * chunk + i) + h + 1)
                    nc.scalar.activation(hidden[:, i % HS, h, :, :], ps_up[h][:, :, :], ACT.Gelu).then_inc(gelu_done, 1)

            for n in range(PIECES):
                k = slice(*FIRST[n])
                act.dma_start(x_raw[:, k, :], x_cols[0:1, :, k, :].rearrange("a p k s -> (a p) k s")).then_inc(first_x_in[n], 16)
            for n in range(PIECES):
                k = slice(*FIRST[n])
                act.wait_ge(first_x_in[n], 16)
                nc.scalar.activation(x_hi[:, 0, k, :], x_raw[:, k, :], ACT.Copy).then_inc(first_x_hi, 1)
                act.wait_ge(first_w_in[n], 16)
                nc.scalar.activation(w_hi[:, 0, k, :], w_raw[:, 0, k, :], ACT.Copy).then_inc(first_w_hi, 1)

            def steps(lora, ffn, more):
                order = plan(lora, ffn)
                waiting = None
                for (kind, i), (then, _) in zip(order, order[1:] + [("", 0)]):
                    if kind == "L":
                        if ffn is not None and i == LEAD:
                            t_high(ffn, 0)
                        if i + 1 < LU:
                            w_high(lora, i + 1)
                        elif more:
                            w_high(lora + 1, 0)
                        x_steps = X_STEPS_FIRST if ffn is None else X_STEPS
                        if i == x_steps[0]:
                            x_high(BC * lora + 1, 1)
                        if i == x_steps[1] and more:
                            x_high(BC * lora + 2, 0)
                        if ffn is None and i in UP_STEPS:
                            heads, own, other = up_half(UP_STEPS.index(i))
                            act.wait_ge(up_in, 16)
                            nc.scalar.activation(up_hi[own, heads, :], up_raw[own, :, :], ACT.Copy).then_inc(up_hi_done, 1)
                        y_copy(lora, i)
                        if then == "F" and not (last_body(lora) and i == LU - 1):
                            waiting = i
                        else:
                            y_park(lora, i)
                    else:
                        if i + 1 < FU:
                            t_high(ffn, i + 1)
                        elif last_body(lora):
                            t_high(ffn + 1, 0)
                        if i == 0 and not isinstance(ffn, int):
                            act.wait_ge(up_lo_own, 2)
                            act.wait_ge(up_lo_other, 2)
                            act.wait_ge(up_hi_other, 2)
                        gelu(ffn, i)
                        if waiting is not None:
                            y_park(lora, waiting)
                            waiting = None

            over_chunks(act, steps)

        @block.vector
        def _(dve):
            def w_low(chunk, i):
                g = LU * chunk + i
                for n in range(2):
                    k = slice(n * HALF, (n + 1) * HALF)
                    dve.wait_ge(w_hi_done, 2 * (g - 1) + n + 1)
                    nc.vector.tensor_tensor(w_lo[:, i % WS, k, :], w_raw[:, i % WRAW, k, :],
                                            w_hi[:, i % WS, k, :].bitcast(F32), ALU.subtract).then_inc(w_lo_done, 1)

            def x_low(b, slot):
                dve.wait_ge(x_hi_done, b)
                nc.vector.tensor_tensor(x_lo[:, slot, :, :], x_raw[:, :, :], x_hi[:, slot, :, :].bitcast(F32),
                                        ALU.subtract).then_inc(x_lo_done, 1)

            def t_low(chunk, i):
                f = FU * chunk + i
                dve.wait_ge(t_hi_done, 2 * (f + 1))
                nc.vector.tensor_tensor(t_split[DH:P, i % SS, 0, :], t_raw[0:DH, i % TG, :],
                                        t_split[0:DH, i % SS, 0, :].bitcast(F32), ALU.subtract)
                nc.vector.tensor_tensor(t_split[0:DH, i % SS, 1, :], t_raw[DH:P, i % TG, :],
                                        t_split[DH:P, i % SS, 1, :].bitcast(F32), ALU.subtract).then_inc(t_lo_done, 1)

            def add_x(chunk, i):
                f = FU * chunk + i
                dve.wait_ge(rows_in[i], 16 * (chunk + 1))
                dve.wait_ge(down_done, f + 1)
                nc.vector.tensor_tensor(rows[:, i, :], ps_dn[i % 2][:, :], rows[:, i, :], ALU.add).then_inc(added, 1)

            for n in range(PIECES):
                k = slice(*FIRST[n])
                dve.wait_ge(first_w_hi, n + 1)
                nc.vector.tensor_tensor(w_lo[:, 0, k, :], w_raw[:, 0, k, :], w_hi[:, 0, k, :].bitcast(F32),
                                        ALU.subtract).then_inc(first_w_lo, 1)

            def steps(lora, ffn, more):
                for kind, i in plan(lora, ffn):
                    if kind == "L":
                        if ffn is not None and i == LEAD:
                            t_low(ffn, 0)
                        if i + 1 < LU:
                            w_low(lora, i + 1)
                        elif more:
                            w_low(lora + 1, 0)
                        x_steps = X_STEPS_FIRST if ffn is None else X_STEPS
                        if i == x_steps[0]:
                            x_low(BC * lora + 1, 1)
                        if i == x_steps[1] and more:
                            x_low(BC * lora + 2, 0)
                        if ffn is None and i in UP_STEPS:
                            half = UP_STEPS.index(i)
                            heads, own, other = up_half(half)
                            dve.wait_ge(up_hi_done, half + 1)
                            nc.vector.tensor_tensor(up_lo[other, heads, :], up_raw[own, :, :],
                                                    up_hi[own, heads, :].bitcast(F32), ALU.subtract).then_inc(up_lo_other, 1)
                            nc.vector.tensor_copy(up_hi[other, heads, :], up_raw[own, :, :]).then_inc(up_hi_other, 1)
                    else:
                        if i + 1 < FU:
                            t_low(ffn, i + 1)
                        elif last_body(lora):
                            t_low(ffn + 1, 0)
                        if i > 0:
                            add_x(ffn, i - 1)
                if ffn is not None:
                    add_x(ffn, FU - 1)

            over_chunks(dve, steps)

        @block.tensor
        def _(pe):
            def first_lora_unit():
                for n in range(PIECES):
                    pe.wait_ge(first_x_lo, n + 1)
                    pe.wait_ge(first_w_lo, n + 1)
                    for o, acc in enumerate((ps_y[0][:, 0, :], ps_dn[0][:, 0:S])):
                        col = slice(o * P, (o + 1) * P)
                        for k in range(*FIRST[n]):
                            nc.tensor.matmul(acc, w_hi[:, 0, k, col], x_hi[:, 0, k, :], start=(k == 0), stop=False)
                            nc.tensor.matmul(acc, w_hi[:, 0, k, col], x_lo[:, 0, k, :], start=False, stop=False)
                            last = nc.tensor.matmul(acc, w_lo[:, 0, k, col], x_hi[:, 0, k, :], start=False, stop=(k == KT - 1))
                last.then_inc(lora_done, 1)

            def lora_unit(chunk, i):
                g = LU * chunk + i
                xs, ws = i // LPB, i % WS
                if i % LPB == 0:
                    pe.wait_ge(x_lo_done, BC * chunk + xs)
                if not isinstance(g, int) or g >= 2:
                    pe.wait_ge(y_copied, g - 1)
                for o in range(OT):
                    col = slice(o * P, (o + 1) * P)
                    for k in range(KT):
                        if o == 0 and k % HALF == 0:
                            pe.wait_ge(w_lo_done, 2 * (g - 1) + k // HALF + 1)
                        acc = ps_y[i % 2][:, o, :]
                        nc.tensor.matmul(acc, w_hi[:, ws, k, col], x_hi[:, xs, k, :], start=(k == 0), stop=False)
                        nc.tensor.matmul(acc, w_hi[:, ws, k, col], x_lo[:, xs, k, :], start=False, stop=False)
                        last = nc.tensor.matmul(acc, w_lo[:, ws, k, col], x_hi[:, xs, k, :], start=False, stop=(k == KT - 1))
                last.then_inc(lora_done, 1)

            def up_unit(chunk, i):
                f = FU * chunk + i
                pe.wait_ge(t_lo_done, f + 1)
                for h in range(2):
                    if i > 0:
                        pe.wait_ge(gelu_done, 2 * (FU * chunk + i - 1) + h + 1)
                    for m in range(MT):
                        col = slice(m * P, (m + 1) * P)
                        nc.tensor.matmul(ps_up[h][:, m, :], up_hi[:, 2 * i + h, col], t_split[:, i % SS, h, :], start=True, stop=False)
                        last = nc.tensor.matmul(ps_up[h][:, m, :], up_lo[:, 2 * i + h, col], t_split[:, i % SS, h, :], start=False, stop=True)
                    last.then_inc(up_done, 1)

            def down_unit(chunk, i):
                f = FU * chunk + i
                pe.wait_ge(gelu_done, 2 * (f + 1))
                if i > 1:
                    pe.wait_ge(added, FU * chunk + i - 1)
                for m in range(MT):
                    for h in range(2):
                        last = nc.tensor.matmul(ps_dn[i % 2][h * DH:(h + 1) * DH, :], down_sb[:, 2 * i + h, m, :],
                                                hidden[:, i % HS, h, m, :], start=(m == 0), stop=(m == MT - 1))
                last.then_inc(down_done, 1)

            def steps(lora, ffn, more):
                for kind, i in plan(lora, ffn):
                    if ffn is None and i == 0:
                        first_lora_unit()
                    elif kind == "L":
                        lora_unit(lora, i)
                    else:
                        if i == 0 and not isinstance(ffn, int):
                            pe.wait_ge(up_lo_own, 2)
                            pe.wait_ge(up_lo_other, 2)
                            pe.wait_ge(up_hi_other, 2)
                            pe.wait_ge(down_in, 16)
                        up_unit(ffn, i)
                        if i > 0:
                            down_unit(ffn, i - 1)
                if ffn is not None:
                    down_unit(ffn, FU - 1)

            over_chunks(pe, steps)


def kernel(x, itok_B_0_15, L0_cond_weight, L0_ffn_up, L0_ffn_down, L0_ffn_perm):
    import concourse.bacc as bacc
    from concourse.bass_utils import run_bass_kernel_spmd

    x, w = np.asarray(x), np.asarray(L0_cond_weight)
    up, down = np.asarray(L0_ffn_up), np.asarray(L0_ffn_down)
    perm, ids = np.asarray(L0_ffn_perm), np.asarray(itok_B_0_15)
    arrays = {
        "x_cols": x.reshape(B, S, KT, P).transpose(0, 3, 2, 1),
        "x_rows": x.reshape(CH, BC, S, D).transpose(0, 3, 1, 2).reshape(CH * D, TOK),
        "w": w.reshape(NW * LPB, OU, KT, P).transpose(0, 3, 2, 1),
        "up": up.reshape(2, H // 2, DH, M).transpose(0, 2, 1, 3).reshape(P, H // 2, M),
        "down": down.reshape(H, MT, P, DH).transpose(2, 0, 1, 3),
        "perm": perm.reshape(FU, P).T,
        "ids": ids.reshape(1, B),
    }
    arrays = {n: np.ascontiguousarray(a) for n, a in arrays.items()}
    nc = bacc.Bacc("TRN2", target_bir_lowering=False, num_devices=1)
    aps = [nc.dram_tensor(n, a.shape, mybir.dt.from_np(a.dtype), kind="ExternalInput").ap() for n, a in arrays.items()]
    out = nc.dram_tensor("out_rows", [CH * D, TOK], F32, kind="ExternalOutput").ap()
    build(nc, *aps, out)
    got = run_bass_kernel_spmd(nc, [arrays], core_ids=[0]).results[0]["out_rows"]
    return got.reshape(CH, D, BC, S).transpose(0, 2, 3, 1).reshape(B, S, D)
```
